# Optimizing a Trainium2 kernel written in Bass

```python
import numpy as np
import jax
import jax.numpy as jnp

def _softmax(x, axis=-1):
    return jax.nn.softmax(x, axis=axis)

def _gelu(x):
    return jax.nn.gelu(x, approximate=True)

def _silu(x):
    return jax.nn.silu(x)

def _sigmoid(x):
    return jax.nn.sigmoid(x)

def _layernorm(x, axis=-1, eps=1e-05):
    m = jnp.mean(x, axis=axis, keepdims=True)
    v = jnp.var(x, axis=axis, keepdims=True)
    return (x - m) / jnp.sqrt(v + eps)

def _scatter_add(tgt, idx, src, axis=0):
    return tgt.at[idx].add(src)

def _segment_sum(src, seg, n):
    return jax.ops.segment_sum(src, seg, n)
kernel_name = 'mk_xattn_seq_d1_seqx_r4_6d6ed5'

def setup_inputs(seed: int=0):
    np.random.seed(seed)
    _w = jnp.asarray

    def _rec_inputs():
        import jax
        import jax.numpy as jnp
        _rk = jax.random.key(seed)
        x = -0.000125 + 0.9999 * jax.random.normal(jax.random.fold_in(_rk, 1), (4, 512, 512), jnp.float32)
        _lenS = 512 - jax.random.randint(jax.random.fold_in(_rk, 7), (4,), 0, max(1, 512 // 4) + 1, jnp.int32)
        _lenS2 = 512 - jax.random.randint(jax.random.fold_in(_rk, 8), (4,), 0, max(1, 512 // 4) + 1, jnp.int32)
        _ctx_1024P = jax.random.normal(jax.random.fold_in(_rk, 11), (4, 16, 256), jnp.float32)
        _ctx_1024c = jax.random.dirichlet(jax.random.fold_in(_rk, 511), 0.3 * jnp.ones((16,), jnp.float32), (4, 512))
        _ctx_1024t = jnp.einsum('bsk,bkd->bsd', _ctx_1024c, _ctx_1024P)
        _ctx_1024t = _ctx_1024t * jax.lax.rsqrt(jnp.mean(jnp.square(_ctx_1024t)) + 1e-12) * 0.953939
        ctx_1024 = 4.13588e-05 + 0.999923 * (_ctx_1024t + 0.3 * jax.random.normal(jax.random.fold_in(_rk, 611), (4, 512, 256), jnp.float32))
        return (x, ctx_1024)
    x, ctx_1024 = _rec_inputs()

    def _L0_xattn_setup():
        import jax, jax.numpy as jnp
        import numpy as np
        EPS = 1e-06

        def _rmsnorm(x, w):
            var = jnp.mean(jnp.square(x), axis=-1, keepdims=True)
            return x * jax.lax.rsqrt(var + EPS) * w
        key = jax.random.key(seed)
        ks = jax.random.split(key, 6)
        B, N, M = (4, 1024, 512)
        d_model, memory_dim = (512, 256)
        hidden_states = jax.random.normal(ks[0], (B, N, d_model), dtype=jnp.float32)
        memory = jax.random.normal(ks[1], (B, M, memory_dim), dtype=jnp.float32)
        W_mem = jax.random.normal(ks[2], (d_model, memory_dim), dtype=jnp.float32) / np.sqrt(memory_dim)
        W_gate = jax.random.normal(ks[3], (d_model, 2 * d_model), dtype=jnp.float32) / np.sqrt(2 * d_model)
        b_gate = jax.random.normal(ks[4], (d_model,), dtype=jnp.float32) * 0.01
        norm_w = jnp.ones((d_model,), dtype=jnp.float32)
        return {'hidden_states': hidden_states, 'memory': memory, 'W_mem': W_mem, 'W_gate': W_gate, 'b_gate': b_gate, 'norm_w': norm_w}
    _L0_xattn_all = _L0_xattn_setup()
    _L0_xattn_in = {k: v for k, v in _L0_xattn_all.items() if k in ('W_mem', 'W_gate', 'b_gate', 'norm_w')}
    del _L0_xattn_all
    return {'x': x, 'ctx_1024': ctx_1024, 'L0_xattn_W_mem': _L0_xattn_in['W_mem'], 'L0_xattn_W_gate': _L0_xattn_in['W_gate'], 'L0_xattn_b_gate': _L0_xattn_in['b_gate'], 'L0_xattn_norm_w': _L0_xattn_in['norm_w']}

def reference(x, ctx_1024, L0_xattn_W_mem, L0_xattn_W_gate, L0_xattn_b_gate, L0_xattn_norm_w):
    import jax
    import jax.numpy as jnp

    def _L0_xattn_ref(hidden_states, memory, W_mem, W_gate, b_gate, norm_w):
        import jax, jax.numpy as jnp
        import numpy as np
        EPS = 1e-06

        def _rmsnorm(x, w):
            var = jnp.mean(jnp.square(x), axis=-1, keepdims=True)
            return x * jax.lax.rsqrt(var + EPS) * w
        D = hidden_states.shape[-1]
        memory_proj = jnp.einsum('bme,de->bmd', memory, W_mem)
        scores = jnp.einsum('bnd,bmd->bnm', hidden_states, memory_proj) / jnp.sqrt(jnp.float32(D))
        attn = jax.nn.softmax(scores, axis=-1)
        memory_context = jnp.einsum('bnm,bmd->bnd', attn, memory_proj)
        gate_input = jnp.concatenate([hidden_states, memory_context], axis=-1)
        gate = jax.nn.sigmoid(jnp.einsum('bnf,df->bnd', gate_input, W_gate) + b_gate)
        fused = hidden_states + gate * memory_context
        return _rmsnorm(fused, norm_w)
    x = _L0_xattn_ref(x, ctx_1024, L0_xattn_W_mem, L0_xattn_W_gate, L0_xattn_b_gate, L0_xattn_norm_w)
    return x

_drawn_inputs = setup_inputs


def setup_inputs(seed=0):
    import zlib

    import numpy as np

    out = dict(_drawn_inputs(seed))
    spreads = {'L0_xattn_norm_w': (1.0, 0.2)}
    factors = {'L0_xattn_b_gate': 50.787}
    for name, (base, spread) in spreads.items():
        noise = np.random.default_rng([zlib.crc32(name.encode()), seed]).standard_normal(out[name].shape)
        drawn = base * np.exp(spread * noise) if base else spread * noise
        out[name] = jnp.asarray(drawn.astype(out[name].dtype))
    for name, factor in factors.items():
        out[name] = (out[name] * factor).astype(out[name].dtype)
    return out
```

```python
from contextlib import ExitStack

import concourse.bass as bass
from concourse import mybir

F32 = mybir.dt.float32
F32R = mybir.dt.float32r
ALU = mybir.AluOpType
ACT = mybir.ActivationFunctionType
AX = mybir.AxisListType

P = 128
EPS = 1e-6


def bass_gated_cross_attention(
    nc: bass.Bass,
    x: bass.AP,
    x_t: bass.AP,
    ctx: bass.AP,
    ctx_t: bass.AP,
    w_mem: bass.AP,
    w_mem_t: bass.AP,
    w_gate_t: bass.AP,
    b_gate: bass.AP,
    norm_w: bass.AP,
    out: bass.AP,
):
    B, N, D = x.shape
    M = ctx_t.shape[3]
    E = w_mem.shape[2]
    KD, KE, KM, TN = D // P, E // P, M // P, N // P
    SCALE = float(D) ** -0.5
    assert N == 512 and M == 512 and D == 512 and KE == 2 and TN == 4 and KM == 4

    with ExitStack() as stack:
        def sb(name, shape, dt=F32):
            return stack.enter_context(nc.sbuf_tensor(name, shape, dt))

        def sem(name):
            return stack.enter_context(nc.semaphore(name))

        def hi_lo(name, shape):
            return sb(name + "_hi", shape, F32R), sb(name + "_lo", shape, F32R)

        xt_raw = sb("xt_raw", [P, KD, N])
        ctxt_raw = sb("ctxt_raw", [P, KE, M])
        ctx_raw = sb("ctx_raw", [P, KM, E])
        wm_raw = sb("wm_raw", [P, KD, E])
        wmt_raw = sb("wmt_raw", [P, KE, D])
        wgt_raw = sb("wgt_raw", [P, 2 * KD, D])
        rows = sb("rows", [P, TN, D])
        bias = sb("bias", [P, D])
        normw = sb("normw", [P, D])
        xt_hi, xt_lo = hi_lo("xt", [P, KD, N])
        ctxt_hi, ctxt_lo = hi_lo("ctxt", [P, KE, M])
        ctx_hi, ctx_lo = hi_lo("ctx", [P, KM, E])
        wm_hi, wm_lo = hi_lo("wm", [P, KD, E])
        wmt_hi, wmt_lo = hi_lo("wmt", [P, KE, D])
        wg1_hi, wg1_lo = hi_lo("wg1", [P, KD, D])
        wg2_hi, wg2_lo = hi_lo("wg2", [P, KD, D])
        wgm_hi, wgm_lo = hi_lo("wgm", [P, KE, D])
        xw_hi, xw_lo = hi_lo("xw", [P, KE, N])
        pt_hi, pt_lo = hi_lo("pt", [P, KM, N])
        ct_hi, ct_lo = hi_lo("ct", [P, KE, N])
        prob = sb("prob", [P, TN, M])
        neg_max = sb("neg_max", [P, TN])
        row_sum = sb("row_sum", [P, TN])
        inv_sum = sb("inv_sum", [P, TN])
        z = sb("z", [P, 2, D])
        v = sb("v", [P, 2, D])
        mean_sq = sb("mean_sq", [P, TN])
        mean_eps = sb("mean_eps", [P, TN])
        rstd = sb("rstd", [P, TN])
        minus_half = sb("minus_half", [P, 1])
        eps = sb("eps", [P, 1])
        ident = sb("ident", [P, P])

        gate = [stack.enter_context(nc.psum_tensor(f"gate{n}", [P, D], F32)) for n in range(TN)]
        work = [stack.enter_context(nc.psum_tensor(f"work{n}", [P, 512], F32)) for n in range(4)]
        xw_bank = [work[0], work[1]]
        tile_bank = [work[2], work[3], work[0], work[1]]
        ct_bank = [work[2], work[3]]
        wgm_bank = [work[0], work[1]]
        context_bank = work

        wm_loaded = [sem(f"wm_loaded{i}") for i in range(2)]
        xt0_loaded = [sem(f"xt0_loaded{k}") for k in range(KD)]
        wgt_loaded = [sem(f"wgt_loaded{i}") for i in range(4)]
        ctxt_loaded = sem("ctxt_loaded")
        ctx_loaded = sem("ctx_loaded")
        wmt_loaded = sem("wmt_loaded")
        xt_loaded = sem("xt_loaded")
        x_loaded = sem("x_loaded")
        bias_loaded = sem("bias_loaded")
        normw_loaded = sem("normw_loaded")
        wm_hi_done = sem("wm_hi_done")
        wm_ready = sem("wm_ready")
        xt_hi_done = sem("xt_hi_done")
        xt_ready = sem("xt_ready")
        wg1_hi_done = sem("wg1_hi_done")
        wg1_ready = sem("wg1_ready")
        ctxt_hi_done = sem("ctxt_hi_done")
        ctxt_ready = sem("ctxt_ready")
        ctx_ready = sem("ctx_ready")
        wmt_ready = sem("wmt_ready")
        wg2_ready = sem("wg2_ready")
        ctx_hi_done = sem("ctx_hi_done")
        wg2_hi_done = sem("wg2_hi_done")
        wmt_hi_done = sem("wmt_hi_done")
        xt_used = sem("xt_used")
        xw_done = sem("xw_done")
        xw_hi_done = sem("xw_hi_done")
        xw_ready = sem("xw_ready")
        scores_done = sem("scores_done")
        max_done = sem("max_done")
        exp_done = sem("exp_done")
        inv_done = sem("inv_done")
        prob_ready = sem("prob_ready")
        pt_done = sem("pt_done")
        pt_hi_done = sem("pt_hi_done")
        pt_ready = sem("pt_ready")
        ct_done = sem("ct_done")
        ct_hi_done = sem("ct_hi_done")
        ct_ready = sem("ct_ready")
        wgm_done = sem("wgm_done")
        wgm_hi_done = sem("wgm_hi_done")
        wgm_ready = sem("wgm_ready")
        gated_done = sem("gated_done")
        z_done = sem("z_done")
        tanh_done = sem("tanh_done")
        v_done = sem("v_done")
        fused_done = sem("fused_done")
        mean_done = sem("mean_done")
        eps_done = sem("eps_done")
        rstd_done = sem("rstd_done")
        rows_done = sem("rows_done")
        stored = [sem(f"stored{n}") for n in range(TN)]
        zero_done = sem("zero_done")
        ident_done = sem("ident_done")
        consts_done = sem("consts_done")

        block = stack.enter_context(nc.Block())

        @block.sync
        def _(sp):
            for i in range(2):
                ks = slice(2 * i, 2 * i + 2)
                sp.dma_start(wm_raw[:, ks, :], w_mem[:, ks, :]).then_inc(wm_loaded[i], 16)
                for k in (2 * i, 2 * i + 1):
                    sp.dma_start(xt_raw[:, k, :], x_t[0, :, k, :]).then_inc(xt0_loaded[k], 16)
            for i in range(2):
                ks = slice(2 * i, 2 * i + 2)
                sp.dma_start(wgt_raw[:, ks, :], w_gate_t[:, ks, :]).then_inc(wgt_loaded[i], 16)
            sp.dma_start(ctxt_raw[:, :, :], ctx_t[0]).then_inc(ctxt_loaded, 16)
            sp.dma_start(ctx_raw[:, :, :], ctx[0]).then_inc(ctx_loaded, 16)
            for i in range(2, 4):
                ks = slice(2 * i, 2 * i + 2)
                sp.dma_start(wgt_raw[:, ks, :], w_gate_t[:, ks, :]).then_inc(wgt_loaded[i], 16)
            sp.dma_start(wmt_raw[:, :, :], w_mem_t).then_inc(wmt_loaded, 16)
            sp.dma_start(bias[:, :], b_gate.partition_broadcast(P)).then_inc(bias_loaded, 16)
            sp.dma_start(rows[:, :, :], x[0].rearrange("(t p) d -> p t d", p=P)).then_inc(x_loaded, 16)
            sp.dma_start(normw[:, :], norm_w.partition_broadcast(P)).then_inc(normw_loaded, 16)

            def store_rows(b):
                for n in range(TN):
                    sp.wait_ge(rows_done, TN * b + n + 1)
                    sp.dma_start(out[b, n * P:(n + 1) * P, :], rows[:, n, :]).then_inc(stored[n], 16)

            with sp.Fori(0, B - 1) as b:
                sp.wait_ge(xt_ready, KD * (b + 1))
                sp.dma_start(xt_raw[:, :, :], x_t[b + 1]).then_inc(xt_loaded, 16)
                sp.wait_ge(ctxt_ready, KE * (b + 1))
                sp.dma_start(ctxt_raw[:, :, :], ctx_t[b + 1]).then_inc(ctxt_loaded, 16)
                sp.wait_ge(ctx_ready, KM * (b + 1))
                sp.dma_start(ctx_raw[:, :, :], ctx[b + 1]).then_inc(ctx_loaded, 16)
                store_rows(b)
                for n in range(TN):
                    sp.wait_ge(stored[n], 16 * (b + 1))
                sp.dma_start(rows[:, :, :], x[b + 1].rearrange("(t p) d -> p t d", p=P))\
                    .then_inc(x_loaded, 16)
            store_rows(B - 1)
            for n in range(TN):
                sp.wait_ge(stored[n], 16 * B)

        @block.gpsimd
        def _(pool):
            nc.gpsimd.memset(ident[:, :], 0.0).then_inc(zero_done, 1)
            nc.gpsimd.memset(minus_half[:, :], -0.5).then_inc(consts_done, 1)
            nc.gpsimd.memset(eps[:, :], EPS).then_inc(consts_done, 1)
            pool.wait_ge(zero_done, 1)
            nc.gpsimd.affine_select(out=ident[:, :], in_=ident[:, :], compare_op=ALU.not_equal, fill=1.0,
                                    base=0, pattern=[[-1, P]], channel_multiplier=1).then_inc(ident_done, 1)

            def remainder(lo, raw, hi, ready, slices):
                nc.gpsimd.tensor_tensor(lo, raw, hi.bitcast(F32), ALU.subtract).then_inc(ready, slices)

            def remainders_of_ctx(b):
                for i in range(2):
                    ks = slice(2 * i, 2 * i + 2)
                    pool.wait_ge(ctx_hi_done, 2 * b + i + 1)
                    remainder(ctx_lo[:, ks, :], ctx_raw[:, ks, :], ctx_hi[:, ks, :], ctx_ready, 2)

            def inverse_rms(b, n):
                pool.wait_ge(mean_done, TN * b + n + 1)
                nc.gpsimd.tensor_tensor(mean_eps[:, n:n + 1], mean_sq[:, n:n + 1], eps[:, :], ALU.add)\
                    .then_inc(eps_done, 1)
                pool.wait_ge(eps_done, TN * b + n + 1)
                nc.gpsimd.tensor_tensor(rstd[:, n:n + 1], mean_eps[:, n:n + 1], minus_half[:, :], ALU.pow)\
                    .then_inc(rstd_done, 1)

            for k in range(KD):
                pool.wait_ge(wgt_loaded[2 + k // 2], 16)
                nc.gpsimd.tensor_copy(wg2_hi[:, k, :], wgt_raw[:, KD + k, :]).then_inc(wg2_hi_done, 1)
                pool.wait_ge(wg2_hi_done, k + 1)
                remainder(wg2_lo[:, k, :], wgt_raw[:, KD + k, :], wg2_hi[:, k, :], wg2_ready, 1)
            remainders_of_ctx(0)
            pool.wait_ge(wmt_loaded, 16)
            for e in range(KE):
                nc.gpsimd.tensor_copy(wmt_hi[:, e, :], wmt_raw[:, e, :]).then_inc(wmt_hi_done, 1)
                pool.wait_ge(wmt_hi_done, e + 1)
                remainder(wmt_lo[:, e, :], wmt_raw[:, e, :], wmt_hi[:, e, :], wmt_ready, 1)

            pool.wait_ge(consts_done, 2)
            with pool.Fori(1, B) as b:
                for e in range(KE):
                    pool.wait_ge(ctxt_hi_done, KE * b + e + 1)
                    remainder(ctxt_lo[:, e, :], ctxt_raw[:, e, :], ctxt_hi[:, e, :], ctxt_ready, 1)
                for k in range(KD):
                    pool.wait_ge(xt_hi_done, KD * b + k + 1)
                    remainder(xt_lo[:, k, :], xt_raw[:, k, :], xt_hi[:, k, :], xt_ready, 1)
                remainders_of_ctx(b)
                for n in range(TN):
                    inverse_rms(b - 1, n)
            for n in range(TN):
                inverse_rms(B - 1, n)

        @block.scalar
        def _(act):
            for k in range(KD):
                if k % 2 == 0:
                    act.wait_ge(wm_loaded[k // 2], 16)
                nc.scalar.activation(wm_hi[:, k, :], wm_raw[:, k, :], ACT.Copy).then_inc(wm_hi_done, 1)
                act.wait_ge(xt0_loaded[k], 16)
                nc.scalar.activation(xt_hi[:, k, :], xt_raw[:, k, :], ACT.Copy).then_inc(xt_hi_done, 1)
            for k in range(KD):
                act.wait_ge(wgt_loaded[k // 2], 16)
                nc.scalar.activation(wg1_hi[:, k, :], wgt_raw[:, k, :], ACT.Copy).then_inc(wg1_hi_done, 1)
            act.wait_ge(ctxt_loaded, 16)
            for e in range(KE):
                nc.scalar.activation(ctxt_hi[:, e, :], ctxt_raw[:, e, :], ACT.Copy).then_inc(ctxt_hi_done, 1)

            def ctx_first_parts(b):
                act.wait_ge(ctx_loaded, 16 * (b + 1))
                for i in range(2):
                    ks = slice(2 * i, 2 * i + 2)
                    nc.scalar.activation(ctx_hi[:, ks, :], ctx_raw[:, ks, :], ACT.Copy).then_inc(ctx_hi_done, 1)

            def next_operands(b):
                act.wait_ge(ctxt_loaded, 16 * (b + 1))
                act.wait_ge(scores_done, TN * b)
                for e in range(KE):
                    nc.scalar.activation(ctxt_hi[:, e, :], ctxt_raw[:, e, :], ACT.Copy)\
                        .then_inc(ctxt_hi_done, 1)
                act.wait_ge(xt_loaded, 16 * b)
                act.wait_ge(xt_used, b)
                for k in range(KD):
                    nc.scalar.activation(xt_hi[:, k, :], xt_raw[:, k, :], ACT.Copy).then_inc(xt_hi_done, 1)

            def tanh(b, n):
                act.wait_ge(z_done, TN * b + n + 1)
                nc.scalar.activation(z[:, n % 2, :], z[:, n % 2, :], ACT.Tanh, scale=0.5)\
                    .then_inc(tanh_done, 1)

            def square(b, n):
                act.wait_ge(fused_done, TN * b + n + 1)
                nc.scalar.activation(v[:, n % 2, :], rows[:, n, :], ACT.Square, scale=SCALE,
                                     accum_out=mean_sq[:, n:n + 1]).then_inc(mean_done, 1)

            def softmax(b):
                for e in range(KE):
                    act.wait_ge(xw_done, KE * b + e + 1)
                    nc.scalar.activation(xw_hi[:, e, :], xw_bank[e][:, :], ACT.Copy, scale=SCALE)\
                        .then_inc(xw_hi_done, 1)
                for n in range(TN):
                    act.wait_ge(max_done, TN * b + n + 1)
                    nc.scalar.activation(prob[:, n, :], tile_bank[n][:, :], ACT.Exp, bias=neg_max[:, n:n + 1],
                                         accum_out=row_sum[:, n:n + 1]).then_inc(exp_done, 1)
                for n in range(TN):
                    act.wait_ge(pt_done, TN * b + n + 1)
                    nc.scalar.activation(pt_hi[:, :, n * P:(n + 1) * P],
                                         tile_bank[n][:, :].rearrange("p (m j) -> p m j", j=P), ACT.Copy)\
                        .then_inc(pt_hi_done, 1)

            def c_first_parts(b):
                for e in range(KE):
                    act.wait_ge(ct_done, KE * b + e + 1)
                    nc.scalar.activation(ct_hi[:, e, :], ct_bank[e][:, :], ACT.Copy).then_inc(ct_hi_done, 1)

            def epilogue(b):
                for n in range(TN):
                    tanh(b, n)
                    if n >= 1:
                        square(b, n - 1)
                square(b, TN - 1)

            ctx_first_parts(0)
            softmax(0)
            with act.Fori(1, B) as b:
                next_operands(b)
                c_first_parts(b - 1)
                ctx_first_parts(b)
                epilogue(b - 1)
                softmax(b)
            c_first_parts(B - 1)
            epilogue(B - 1)

        @block.tensor
        def _(pe):
            def product(bank, w_hi, w_lo, m_hi, m_lo, start, stop):
                nc.tensor.matmul(bank, w_hi, m_hi, start=start, stop=False)
                nc.tensor.matmul(bank, w_hi, m_lo, start=False, stop=False)
                return nc.tensor.matmul(bank, w_lo, m_hi, start=False, stop=stop)

            def xw_part(e, k):
                es = slice(e * P, (e + 1) * P)
                return product(xw_bank[e][:, :], wm_hi[:, k, es], wm_lo[:, k, es],
                               xt_hi[:, k, :], xt_lo[:, k, :], k == 0, k == KD - 1)

            def first_xw():
                for k in range(KD):
                    pe.wait_ge(wm_ready, k + 1)
                    pe.wait_ge(xt_ready, k + 1)
                    for e in range(KE):
                        last = xw_part(e, k)
                        if k == KD - 1:
                            last.then_inc(xw_done, 1)

            def xw(b):
                pe.wait_ge(xt_ready, KD * (b + 1))
                for e in range(KE):
                    pe.wait_ge(v_done, TN * (b - 1) + e + 1)
                    for k in range(KD):
                        last = xw_part(e, k)
                    last.then_inc(xw_done, 1)

            def gate_x(b, n, first):
                ns = slice(n * P, (n + 1) * P)
                if not first:
                    pe.wait_ge(z_done, TN * (b - 1) + n + 1)
                for k in range(KD):
                    if first and n == 0:
                        pe.wait_ge(wg1_ready, k + 1)
                    last = product(gate[n][:, :], xt_hi[:, k, ns], xt_lo[:, k, ns],
                                   wg1_hi[:, k, :], wg1_lo[:, k, :], k == 0, False)
                if n == TN - 1:
                    last.then_inc(xt_used, 1)

            def scores(b, n, first):
                ns = slice(n * P, (n + 1) * P)
                if n == 0:
                    pe.wait_ge(xw_ready, KE * (b + 1))
                    pe.wait_ge(ctxt_ready, KE * (b + 1))
                if n < 2 and not first:
                    pe.wait_ge(v_done, TN * (b - 1) + n + 3)
                for e in range(KE):
                    last = product(tile_bank[n][:, :], xw_hi[:, e, ns], xw_lo[:, e, ns],
                                   ctxt_hi[:, e, :], ctxt_lo[:, e, :], e == 0, e == KE - 1)
                last.then_inc(scores_done, 1)

            def transposes(b, n):
                pe.wait_ge(prob_ready, TN * b + n + 1)
                for m in range(KM):
                    ms = slice(m * P, (m + 1) * P)
                    last = nc.tensor.transpose(tile_bank[n][:, ms], prob[:, n, ms], ident[:, :])
                last.then_inc(pt_done, 1)

            def attend_ctx(b, first):
                pe.wait_ge(pt_ready, TN * (b + 1))
                pe.wait_ge(ctx_ready, KM * (b + 1))
                for e in range(KE):
                    es = slice(e * P, (e + 1) * P)
                    for m in range(KM):
                        last = product(ct_bank[e][:, :], ctx_hi[:, m, es], ctx_lo[:, m, es],
                                       pt_hi[:, m, :], pt_lo[:, m, :], m == 0, m == KM - 1)
                    last.then_inc(ct_done, 1)

            def gate_weights():
                for e in range(KE):
                    es = slice(e * P, (e + 1) * P)
                    for k in range(KD):
                        if e == 0:
                            pe.wait_ge(wg2_ready, k + 1)
                        last = product(wgm_bank[e][:, :], wm_hi[:, k, es], wm_lo[:, k, es],
                                       wg2_hi[:, k, :], wg2_lo[:, k, :], k == 0, k == KD - 1)
                    last.then_inc(wgm_done, 1)

            def context_and_gate(b, n, first):
                ns = slice(n * P, (n + 1) * P)
                for e in range(KE):
                    if n == 0:
                        pe.wait_ge(ct_ready, KE * b + e + 1)
                        if first:
                            pe.wait_ge(wmt_ready, e + 1)
                            pe.wait_ge(wgm_ready, e + 1)
                    product(context_bank[n][:, :], ct_hi[:, e, ns], ct_lo[:, e, ns],
                            wmt_hi[:, e, :], wmt_lo[:, e, :], e == 0, e == KE - 1)
                    last = product(gate[n][:, :], ct_hi[:, e, ns], ct_lo[:, e, ns],
                                   wgm_hi[:, e, :], wgm_lo[:, e, :], False, e == KE - 1)
                last.then_inc(gated_done, 1)

            def batch(b, first):
                gate_x(b, 0, first)
                for n in range(TN):
                    scores(b, n, first)
                gate_x(b, 1, first)
                if first:
                    pe.wait_ge(ident_done, 1)
                transposes(b, 0)
                transposes(b, 1)
                gate_x(b, 2, first)
                transposes(b, 2)
                transposes(b, 3)
                gate_x(b, 3, first)
                attend_ctx(b, first)
                if first:
                    gate_weights()
                for n in range(TN):
                    context_and_gate(b, n, first)

            first_xw()
            batch(0, True)
            with pe.Fori(1, B) as b:
                xw(b)
                batch(b, False)

        @block.vector
        def _(dve):
            def remainder(lo, whole, hi, done):
                nc.vector.tensor_tensor(lo, whole, hi.bitcast(F32), ALU.subtract).then_inc(done, 1)

            for k in range(KD):
                dve.wait_ge(wm_hi_done, k + 1)
                remainder(wm_lo[:, k, :], wm_raw[:, k, :], wm_hi[:, k, :], wm_ready)
                dve.wait_ge(xt_hi_done, k + 1)
                remainder(xt_lo[:, k, :], xt_raw[:, k, :], xt_hi[:, k, :], xt_ready)
            for k in range(KD):
                dve.wait_ge(wg1_hi_done, k + 1)
                remainder(wg1_lo[:, k, :], wgt_raw[:, k, :], wg1_hi[:, k, :], wg1_ready)
            for e in range(KE):
                dve.wait_ge(ctxt_hi_done, e + 1)
                remainder(ctxt_lo[:, e, :], ctxt_raw[:, e, :], ctxt_hi[:, e, :], ctxt_ready)

            def row_max(b, n):
                dve.wait_ge(scores_done, TN * b + n + 1)
                nc.vector.tensor_reduce(neg_max[:, n:n + 1], tile_bank[n][:, :], AX.X, ALU.max, negate=True)\
                    .then_inc(max_done, 1)

            def normalise(b, n):
                dve.wait_ge(exp_done, TN * b + n + 1)
                nc.vector.reciprocal(inv_sum[:, n:n + 1], row_sum[:, n:n + 1]).then_inc(inv_done, 1)
                dve.wait_ge(inv_done, TN * b + n + 1)
                nc.vector.tensor_scalar(prob[:, n, :], prob[:, n, :], inv_sum[:, n:n + 1], None, ALU.mult)\
                    .then_inc(prob_ready, 1)

            def gate_sum(b, n):
                dve.wait_ge(gated_done, TN * b + n + 1)
                nc.vector.tensor_tensor(z[:, n % 2, :], gate[n][:, :], bias[:, :], ALU.add).then_inc(z_done, 1)

            def gated_context(b, n):
                dve.wait_ge(tanh_done, TN * b + n + 1)
                nc.vector.scalar_tensor_tensor(out=v[:, n % 2, :], in0=z[:, n % 2, :], scalar=1.0,
                                               in1=context_bank[n][:, :], op0=ALU.add, op1=ALU.mult)\
                    .then_inc(v_done, 1)
                if n == 0:
                    dve.wait_ge(x_loaded, 16 * (b + 1))
                dve.wait_ge(v_done, TN * b + n + 1)
                nc.vector.scalar_tensor_tensor(out=rows[:, n, :], in0=v[:, n % 2, :], scalar=0.5,
                                               in1=rows[:, n, :], op0=ALU.mult, op1=ALU.add)\
                    .then_inc(fused_done, 1)

            def scaled_rows(b, n):
                dve.wait_ge(rstd_done, TN * b + n + 1)
                nc.vector.scalar_tensor_tensor(out=rows[:, n, :], in0=rows[:, n, :], scalar=rstd[:, n:n + 1],
                                               in1=normw[:, :], op0=ALU.mult, op1=ALU.mult)\
                    .then_inc(rows_done, 1)

            def attend(b, first):
                for e in range(KE):
                    dve.wait_ge(xw_hi_done, KE * b + e + 1)
                    nc.vector.scalar_tensor_tensor(out=xw_lo[:, e, :], in0=xw_bank[e][:, :], scalar=SCALE,
                                                   in1=xw_hi[:, e, :].bitcast(F32), op0=ALU.mult,
                                                   op1=ALU.subtract).then_inc(xw_ready, 1)
                row_max(b, 0)
                for n in range(1, TN):
                    row_max(b, n)
                    normalise(b, n - 1)
                normalise(b, TN - 1)
                for n in range(TN):
                    dve.wait_ge(pt_hi_done, TN * b + n + 1)
                    ns = slice(n * P, (n + 1) * P)
                    remainder(pt_lo[:, :, ns], tile_bank[n][:, :].rearrange("p (m j) -> p m j", j=P),
                              pt_hi[:, :, ns], pt_ready)
                for e in range(KE):
                    dve.wait_ge(ct_hi_done, KE * b + e + 1)
                    remainder(ct_lo[:, e, :], ct_bank[e][:, :], ct_hi[:, e, :], ct_ready)
                if first:
                    for e in range(KE):
                        dve.wait_ge(wgm_done, e + 1)
                        nc.vector.tensor_copy(wgm_hi[:, e, :], wgm_bank[e][:, :]).then_inc(wgm_hi_done, 1)
                        dve.wait_ge(wgm_hi_done, e + 1)
                        remainder(wgm_lo[:, e, :], wgm_bank[e][:, :], wgm_hi[:, e, :], wgm_ready)
                    dve.wait_ge(bias_loaded, 16)
                    dve.wait_ge(normw_loaded, 16)
                for n in range(TN):
                    gate_sum(b, n)
                    if n >= 1:
                        gated_context(b, n - 1)
                    if n >= 2:
                        scaled_rows(b, n - 2)
                gated_context(b, TN - 1)
                scaled_rows(b, TN - 2)
                scaled_rows(b, TN - 1)

            attend(0, True)
            with dve.Fori(1, B) as b:
                attend(b, False)


def kernel(x, ctx_1024, L0_xattn_W_mem, L0_xattn_W_gate, L0_xattn_b_gate, L0_xattn_norm_w):
    import numpy as _np
    import concourse.bacc as _bacc
    from concourse import mybir as _mybir
    from concourse.bass_utils import run_bass_kernel_spmd as _run

    x, ctx, w_mem, w_gate = (_np.asarray(a) for a in (x, ctx_1024, L0_xattn_W_mem, L0_xattn_W_gate))

    def over_partitions(a):
        return _np.ascontiguousarray(a.reshape(*a.shape[:-2], -1, 128, a.shape[-1]).swapaxes(-3, -2))

    arrays = {
        "x_dram": _np.ascontiguousarray(x),
        "x_t_dram": over_partitions(x.swapaxes(1, 2)),
        "ctx_dram": over_partitions(ctx),
        "ctx_t_dram": over_partitions(ctx.swapaxes(1, 2)),
        "w_mem_dram": over_partitions(w_mem),
        "w_mem_t_dram": over_partitions(w_mem.T),
        "w_gate_t_dram": over_partitions(w_gate.T),
        "b_gate_dram": _np.ascontiguousarray(L0_xattn_b_gate),
        "norm_w_dram": _np.ascontiguousarray(L0_xattn_norm_w),
    }
    nc = _bacc.Bacc("TRN2", target_bir_lowering=False, num_devices=1)
    args = [nc.dram_tensor(n, a.shape, _mybir.dt.from_np(a.dtype), kind="ExternalInput").ap()
            for n, a in arrays.items()]
    args.append(nc.dram_tensor("out_dram", x.shape, _mybir.dt.float32, kind="ExternalOutput").ap())
    bass_gated_cross_attention(nc, *args)
    r = _run(nc, [arrays], core_ids=[0])
    return r.results[0]["out_dram"]
```

```python
from contextlib import ExitStack

import concourse.bass as bass
from concourse import mybir

F32 = mybir.dt.float32
F32R = mybir.dt.float32r
BF16 = mybir.dt.bfloat16
ALU = mybir.AluOpType
ACT = mybir.ActivationFunctionType
AX = mybir.AxisListType

P = 128
EPS = 1e-6


def bass_gated_cross_attention(
    nc: bass.Bass,
    x: bass.AP,
    x_t: bass.AP,
    ctx: bass.AP,
    ctx_t: bass.AP,
    w_mem: bass.AP,
    w_mem_t: bass.AP,
    w_gate_t: bass.AP,
    b_gate: bass.AP,
    norm_w: bass.AP,
    out: bass.AP,
):
    B, N, D = x.shape
    M = ctx_t.shape[3]
    E = w_mem.shape[2]
    KD, KE, KM, TN = D // P, E // P, M // P, N // P
    SCALE = float(D) ** -0.5
    TILES = [(n, slice(0, D)) for n in range(TN)]
    LAST_PIECES = TILES[:-1] + [(TN - 1, slice(0, D // 2)), (TN - 1, slice(D // 2, D))]
    POOL_FUSED = 3
    DVE_FUSED = TN - POOL_FUSED

    def pieces(b):
        return LAST_PIECES if isinstance(b, int) and b == B - 1 else TILES

    assert N == 512 and M == 512 and D == 512 and KE == 2 and TN == 4 and KM == 4

    with ExitStack() as stack:
        def sb(name, shape, dt=F32):
            return stack.enter_context(nc.sbuf_tensor(name, shape, dt))

        def sem(name):
            return stack.enter_context(nc.semaphore(name))

        def hi_lo(name, shape):
            return sb(name + "_hi", shape, F32R), sb(name + "_lo", shape, F32R)

        xt_raw = sb("xt_raw", [P, KD, N])
        ctxt_raw = sb("ctxt_raw", [P, KE, M])
        ctx_raw = sb("ctx_raw", [P, KM, E])
        wm_raw = sb("wm_raw", [P, KD, E])
        wmt_raw = sb("wmt_raw", [P, KE, D])
        wgt_raw = sb("wgt_raw", [P, 2 * KD, D])
        rows = sb("rows", [P, TN, D])
        bias = sb("bias", [P, D])
        normw = sb("normw", [P, D])
        xt_hi, xt_lo = hi_lo("xt", [P, KD, N])
        ctxt_hi, ctxt_lo = hi_lo("ctxt", [P, KE, M])
        ctx_hi, ctx_lo = hi_lo("ctx", [P, KM, E])
        wm_hi, wm_lo = hi_lo("wm", [P, KD, E])
        wmt_hi, wmt_lo = hi_lo("wmt", [P, KE, D])
        wg1_hi, wg1_lo = hi_lo("wg1", [P, KD, D])
        wg2_hi, wg2_lo = hi_lo("wg2", [P, KD, D])
        wgm_hi, wgm_lo = hi_lo("wgm", [P, KE, D])
        xw_hi, xw_lo = hi_lo("xw", [P, KE, N])
        pt_hi, pt_lo = hi_lo("pt", [P, KM, N])
        ct_hi, ct_lo = hi_lo("ct", [P, KE, N])
        prob = sb("prob", [P, TN, M])
        neg_max = sb("neg_max", [P, TN])
        row_sum = sb("row_sum", [P, TN])
        inv_sum = sb("inv_sum", [P, TN])
        z = sb("z", [P, 2, D])
        v = sb("v", [P, 2, D])
        mean_sq = sb("mean_sq", [P, len(LAST_PIECES)])
        mean_eps = sb("mean_eps", [P, len(LAST_PIECES)])
        rstd = sb("rstd", [P, TN])
        minus_half = sb("minus_half", [P, 1])
        eps = sb("eps", [P, 1])
        ident = sb("ident", [P, P])
        warm = sb("warm", [P, 512], BF16)

        gate = [stack.enter_context(nc.psum_tensor(f"gate{n}", [P, D], F32)) for n in range(TN)]
        work = [stack.enter_context(nc.psum_tensor(f"work{n}", [P, 512], F32)) for n in range(4)]
        xw_bank = [work[0], work[1]]
        tile_bank = [work[2], work[3], work[0], work[1]]
        ct_bank = [work[2], work[3]]
        wgm_bank = [work[0], work[1]]
        context_bank = [work[0], work[1], work[2], work[3], work[1]]

        wm_loaded = [sem(f"wm_loaded{i}") for i in range(3)]
        xt0_loaded = [sem(f"xt0_loaded{k}") for k in range(KD)]
        wgt_loaded = [sem(f"wgt_loaded{i}") for i in range(4)]
        ctxt_loaded = sem("ctxt_loaded")
        ctx_loaded = sem("ctx_loaded")
        wmt_loaded = sem("wmt_loaded")
        xt_loaded = sem("xt_loaded")
        x_loaded = sem("x_loaded")
        bias_loaded = sem("bias_loaded")
        normw_loaded = sem("normw_loaded")
        wm_hi_done = sem("wm_hi_done")
        wm_ready = sem("wm_ready")
        xt_hi_done = sem("xt_hi_done")
        xt_ready = sem("xt_ready")
        wg1_hi_done = sem("wg1_hi_done")
        wg1_ready = sem("wg1_ready")
        ctxt_hi_done = sem("ctxt_hi_done")
        ctxt_ready = sem("ctxt_ready")
        ctx_ready = sem("ctx_ready")
        wmt_ready = sem("wmt_ready")
        wg2_ready = sem("wg2_ready")
        ctx_hi_done = sem("ctx_hi_done")
        wg2_hi_done = sem("wg2_hi_done")
        wmt_hi_done = sem("wmt_hi_done")
        xt_used = sem("xt_used")
        xw_done = sem("xw_done")
        xw_hi_done = sem("xw_hi_done")
        xw_ready = sem("xw_ready")
        scores_done = sem("scores_done")
        max_done = sem("max_done")
        exp_done = sem("exp_done")
        inv_done = sem("inv_done")
        prob_ready = sem("prob_ready")
        pt_done = sem("pt_done")
        pt_hi_done = sem("pt_hi_done")
        pt_ready = sem("pt_ready")
        ct_done = sem("ct_done")
        ct_hi_done = sem("ct_hi_done")
        ct_ready = sem("ct_ready")
        wgm_done = sem("wgm_done")
        wgm_hi_done = sem("wgm_hi_done")
        wgm_ready = sem("wgm_ready")
        gate_done = sem("gate_done")
        context_done = sem("context_done")
        z_done = sem("z_done")
        tanh_done = sem("tanh_done")
        v_done = sem("v_done")
        pool_fused_done = sem("pool_fused_done")
        fused_done = sem("fused_done")
        mean_done = sem("mean_done")
        eps_done = sem("eps_done")
        rstd_done = sem("rstd_done")
        rows_done = sem("rows_done")
        stored = [sem(f"stored{i}") for i in range(len(LAST_PIECES))]
        zero_done = sem("zero_done")
        ident_done = sem("ident_done")
        warm_done = sem("warm_done")
        consts_done = sem("consts_done")

        WARM_UP = 8
        WM_LOADS = [slice(0, 1), slice(1, 2), slice(2, 4)]

        block = stack.enter_context(nc.Block())

        @block.sync
        def _(sp):
            for k in range(KD):
                sp.dma_start(xt_raw[:, k, :], x_t[0, :, k, :]).then_inc(xt0_loaded[k], 16)
                if k < len(WM_LOADS):
                    ks = WM_LOADS[k]
                    sp.dma_start(wm_raw[:, ks, :], w_mem[:, ks, :]).then_inc(wm_loaded[k], 16)
            for i in range(2):
                ks = slice(2 * i, 2 * i + 2)
                sp.dma_start(wgt_raw[:, ks, :], w_gate_t[:, ks, :]).then_inc(wgt_loaded[i], 16)
            sp.dma_start(ctxt_raw[:, :, :], ctx_t[0]).then_inc(ctxt_loaded, 16)
            sp.dma_start(ctx_raw[:, :, :], ctx[0]).then_inc(ctx_loaded, 16)
            for i in range(2, 4):
                ks = slice(2 * i, 2 * i + 2)
                sp.dma_start(wgt_raw[:, ks, :], w_gate_t[:, ks, :]).then_inc(wgt_loaded[i], 16)
            sp.dma_start(wmt_raw[:, :, :], w_mem_t).then_inc(wmt_loaded, 16)
            sp.dma_start(bias[:, :], b_gate.partition_broadcast(P)).then_inc(bias_loaded, 16)
            sp.dma_start(rows[:, :, :], x[0].rearrange("(t p) d -> p t d", p=P)).then_inc(x_loaded, 16)
            sp.dma_start(normw[:, :], norm_w.partition_broadcast(P)).then_inc(normw_loaded, 16)

            def store_rows(b):
                for i, (n, cols) in enumerate(pieces(b)):
                    sp.wait_ge(rows_done, TN * b + i + 1)
                    sp.dma_start(out[b, n * P:(n + 1) * P, cols], rows[:, n, cols]).then_inc(stored[i], 16)

            with sp.Fori(0, B - 1) as b:
                sp.wait_ge(xt_ready, KD * (b + 1))
                sp.dma_start(xt_raw[:, :, :], x_t[b + 1]).then_inc(xt_loaded, 16)
                sp.wait_ge(ctxt_ready, KE * (b + 1))
                sp.dma_start(ctxt_raw[:, :, :], ctx_t[b + 1]).then_inc(ctxt_loaded, 16)
                sp.wait_ge(ctx_ready, KM * (b + 1))
                sp.dma_start(ctx_raw[:, :, :], ctx[b + 1]).then_inc(ctx_loaded, 16)
                store_rows(b)
                for i in range(TN):
                    sp.wait_ge(stored[i], 16 * (b + 1))
                sp.dma_start(rows[:, :, :], x[b + 1].rearrange("(t p) d -> p t d", p=P))\
                    .then_inc(x_loaded, 16)
            store_rows(B - 1)
            for i in range(TN):
                sp.wait_ge(stored[i], 16 * B)
            sp.wait_ge(stored[TN], 16)

        @block.gpsimd
        def _(pool):
            nc.gpsimd.memset(ident[:, :], 0.0).then_inc(zero_done, 1)
            nc.gpsimd.memset(minus_half[:, :], -0.5).then_inc(consts_done, 1)
            nc.gpsimd.memset(eps[:, :], EPS).then_inc(consts_done, 1)
            pool.wait_ge(zero_done, 1)
            nc.gpsimd.affine_select(out=ident[:, :], in_=ident[:, :], compare_op=ALU.not_equal, fill=1.0,
                                    base=0, pattern=[[-1, P]], channel_multiplier=1).then_inc(ident_done, 1)

            def remainder(lo, raw, hi, ready, slices):
                nc.gpsimd.tensor_tensor(lo, raw, hi.bitcast(F32), ALU.subtract).then_inc(ready, slices)

            def remainders_of_ctx(b):
                for i in range(2):
                    ks = slice(2 * i, 2 * i + 2)
                    pool.wait_ge(ctx_hi_done, 2 * b + i + 1)
                    remainder(ctx_lo[:, ks, :], ctx_raw[:, ks, :], ctx_hi[:, ks, :], ctx_ready, 2)

            def remainders_of_ctxt(b):
                for e in range(KE):
                    pool.wait_ge(ctxt_hi_done, KE * b + e + 1)
                    remainder(ctxt_lo[:, e, :], ctxt_raw[:, e, :], ctxt_hi[:, e, :], ctxt_ready, 1)

            def fuse(b, i):
                n, cols = TILES[i]
                if i == 0:
                    pool.wait_ge(x_loaded, 16 * (b + 1))
                pool.wait_ge(v_done, TN * b + i + 1)
                nc.gpsimd.tensor_tensor(rows[:, n, cols], v[:, n % 2, cols], rows[:, n, cols], ALU.add)\
                    .then_inc(pool_fused_done, 1)

            def finish_rows(b):
                fuse(b, 0)
                for i, (n, cols) in enumerate(pieces(b)):
                    if i + 1 < POOL_FUSED:
                        fuse(b, i + 1)
                    before = eps[:, :] if cols.start == 0 else mean_eps[:, i - 1:i]
                    pool.wait_ge(mean_done, TN * b + i + 1)
                    if cols.start > 0:
                        pool.wait_ge(eps_done, TN * b + i)
                    nc.gpsimd.tensor_tensor(mean_eps[:, i:i + 1], mean_sq[:, i:i + 1], before, ALU.add)\
                        .then_inc(eps_done, 1)
                    if cols.stop == D:
                        pool.wait_ge(eps_done, TN * b + i + 1)
                        nc.gpsimd.tensor_tensor(rstd[:, n:n + 1], mean_eps[:, i:i + 1], minus_half[:, :],
                                                ALU.pow).then_inc(rstd_done, 1)

            remainders_of_ctxt(0)
            for k in range(KD):
                pool.wait_ge(wg2_hi_done, k + 1)
                remainder(wg2_lo[:, k, :], wgt_raw[:, KD + k, :], wg2_hi[:, k, :], wg2_ready, 1)
            remainders_of_ctx(0)

            pool.wait_ge(consts_done, 2)
            with pool.Fori(1, B) as b:
                remainders_of_ctxt(b)
                for k in range(KD):
                    pool.wait_ge(xt_hi_done, KD * b + k + 1)
                    remainder(xt_lo[:, k, :], xt_raw[:, k, :], xt_hi[:, k, :], xt_ready, 1)
                remainders_of_ctx(b)
                finish_rows(b - 1)
            finish_rows(B - 1)

        @block.scalar
        def _(act):
            for k in range(KD):
                act.wait_ge(xt0_loaded[k], 16)
                nc.scalar.activation(xt_hi[:, k, :], xt_raw[:, k, :], ACT.Copy).then_inc(xt_hi_done, 1)
                act.wait_ge(wm_loaded[min(k, 2)], 16)
                nc.scalar.activation(wm_hi[:, k, :], wm_raw[:, k, :], ACT.Copy).then_inc(wm_hi_done, 1)
            for k in range(KD):
                act.wait_ge(wgt_loaded[k // 2], 16)
                nc.scalar.activation(wg1_hi[:, k, :], wgt_raw[:, k, :], ACT.Copy).then_inc(wg1_hi_done, 1)
            act.wait_ge(ctxt_loaded, 16)
            for e in range(KE):
                nc.scalar.activation(ctxt_hi[:, e, :], ctxt_raw[:, e, :], ACT.Copy).then_inc(ctxt_hi_done, 1)

            def ctx_first_parts(b):
                act.wait_ge(ctx_loaded, 16 * (b + 1))
                for i in range(2):
                    ks = slice(2 * i, 2 * i + 2)
                    nc.scalar.activation(ctx_hi[:, ks, :], ctx_raw[:, ks, :], ACT.Copy).then_inc(ctx_hi_done, 1)

            def next_operands(b):
                act.wait_ge(ctxt_loaded, 16 * (b + 1))
                act.wait_ge(scores_done, TN * b)
                for e in range(KE):
                    nc.scalar.activation(ctxt_hi[:, e, :], ctxt_raw[:, e, :], ACT.Copy)\
                        .then_inc(ctxt_hi_done, 1)
                act.wait_ge(xt_loaded, 16 * b)
                act.wait_ge(xt_used, b)
                for k in range(KD):
                    nc.scalar.activation(xt_hi[:, k, :], xt_raw[:, k, :], ACT.Copy).then_inc(xt_hi_done, 1)

            def tanh(b, n):
                act.wait_ge(z_done, TN * b + n + 1)
                nc.scalar.activation(z[:, n % 2, :], z[:, n % 2, :], ACT.Tanh, scale=0.5)\
                    .then_inc(tanh_done, 1)

            def square(b, i):
                n, cols = pieces(b)[i]
                if i < POOL_FUSED:
                    act.wait_ge(pool_fused_done, POOL_FUSED * b + i + 1)
                else:
                    act.wait_ge(fused_done, DVE_FUSED * b + i - POOL_FUSED + 1)
                nc.scalar.activation(v[:, n % 2, cols], rows[:, n, cols], ACT.Square, scale=SCALE,
                                     accum_out=mean_sq[:, i:i + 1]).then_inc(mean_done, 1)

            def softmax(b, first):
                for e in range(KE):
                    act.wait_ge(xw_done, KE * b + e + 1)
                    nc.scalar.activation(xw_hi[:, e, :], xw_bank[e][:, :], ACT.Copy, scale=SCALE)\
                        .then_inc(xw_hi_done, 1)
                for n in range(TN):
                    act.wait_ge(max_done, TN * b + n + 1)
                    nc.scalar.activation(prob[:, n, :], tile_bank[n][:, :], ACT.Exp, bias=neg_max[:, n:n + 1],
                                         accum_out=row_sum[:, n:n + 1]).then_inc(exp_done, 1)
                    if first:
                        act.wait_ge(wgt_loaded[2 + n // 2], 16)
                        nc.scalar.activation(wg2_hi[:, n, :], wgt_raw[:, KD + n, :], ACT.Copy)\
                            .then_inc(wg2_hi_done, 1)
                for n in range(TN):
                    act.wait_ge(pt_done, TN * b + n + 1)
                    nc.scalar.activation(pt_hi[:, :, n * P:(n + 1) * P],
                                         tile_bank[n][:, :].rearrange("p (m j) -> p m j", j=P), ACT.Copy)\
                        .then_inc(pt_hi_done, 1)
                if first:
                    act.wait_ge(wmt_loaded, 16)
                    for e in range(KE):
                        nc.scalar.activation(wmt_hi[:, e, :], wmt_raw[:, e, :], ACT.Copy, scale=0.5)\
                            .then_inc(wmt_hi_done, 1)

            def c_first_parts(b):
                for e in range(KE):
                    act.wait_ge(ct_done, KE * b + e + 1)
                    nc.scalar.activation(ct_hi[:, e, :], ct_bank[e][:, :], ACT.Copy).then_inc(ct_hi_done, 1)

            def epilogue(b):
                tanh(b, 0)
                tanh(b, 1)
                square(b, 0)
                tanh(b, 2)
                square(b, 1)
                tanh(b, 3)
                square(b, 2)
                for i in range(3, len(pieces(b))):
                    square(b, i)

            ctx_first_parts(0)
            softmax(0, True)
            with act.Fori(1, B) as b:
                next_operands(b)
                c_first_parts(b - 1)
                ctx_first_parts(b)
                epilogue(b - 1)
                softmax(b, False)
            c_first_parts(B - 1)
            epilogue(B - 1)

        @block.tensor
        def _(pe):
            def product(bank, w_hi, w_lo, m_hi, m_lo, start, stop):
                nc.tensor.matmul(bank, w_hi, m_hi, start=start, stop=False)
                nc.tensor.matmul(bank, w_hi, m_lo, start=False, stop=False)
                return nc.tensor.matmul(bank, w_lo, m_hi, start=False, stop=stop)

            def xw_part(e, k):
                es = slice(e * P, (e + 1) * P)
                return product(xw_bank[e][:, :], wm_hi[:, k, es], wm_lo[:, k, es],
                               xt_hi[:, k, :], xt_lo[:, k, :], k == 0, k == KD - 1)

            def first_xw():
                for k in range(KD):
                    pe.wait_ge(wm_hi_done, k + 1)
                    pe.wait_ge(xt_hi_done, k + 1)
                    for e in range(KE):
                        es = slice(e * P, (e + 1) * P)
                        nc.tensor.matmul(xw_bank[e][:, :], wm_hi[:, k, es], xt_hi[:, k, :],
                                         start=k == 0, stop=False)
                    pe.wait_ge(xt_ready, k + 1)
                    for e in range(KE):
                        es = slice(e * P, (e + 1) * P)
                        nc.tensor.matmul(xw_bank[e][:, :], wm_hi[:, k, es], xt_lo[:, k, :],
                                         start=False, stop=False)
                    pe.wait_ge(wm_ready, k + 1)
                    for e in range(KE):
                        es = slice(e * P, (e + 1) * P)
                        last = nc.tensor.matmul(xw_bank[e][:, :], wm_lo[:, k, es], xt_hi[:, k, :],
                                                start=False, stop=k == KD - 1)
                        if k == KD - 1:
                            last.then_inc(xw_done, 1)

            def xw(b):
                pe.wait_ge(xt_ready, KD * (b + 1))
                for e in range(KE):
                    pe.wait_ge(v_done, TN * (b - 1) + e + 1)
                    for k in range(KD):
                        last = xw_part(e, k)
                    last.then_inc(xw_done, 1)

            def gate_x(b, n, first):
                ns = slice(n * P, (n + 1) * P)
                if not first:
                    pe.wait_ge(z_done, TN * (b - 1) + n + 1)
                for k in range(KD):
                    if first and n == 0:
                        pe.wait_ge(wg1_ready, k + 1)
                    last = product(gate[n][:, :], xt_hi[:, k, ns], xt_lo[:, k, ns],
                                   wg1_hi[:, k, :], wg1_lo[:, k, :], k == 0, False)
                if n == TN - 1:
                    last.then_inc(xt_used, 1)

            def scores(b, n, first):
                ns = slice(n * P, (n + 1) * P)
                if n == 0:
                    pe.wait_ge(xw_ready, KE * (b + 1))
                    pe.wait_ge(ctxt_ready, KE * (b + 1))
                if n < 2 and not first:
                    pe.wait_ge(v_done, TN * (b - 1) + n + 3)
                for e in range(KE):
                    last = product(tile_bank[n][:, :], xw_hi[:, e, ns], xw_lo[:, e, ns],
                                   ctxt_hi[:, e, :], ctxt_lo[:, e, :], e == 0, e == KE - 1)
                last.then_inc(scores_done, 1)

            def transposes(b, n):
                pe.wait_ge(prob_ready, TN * b + n + 1)
                for m in range(KM):
                    ms = slice(m * P, (m + 1) * P)
                    last = nc.tensor.transpose(tile_bank[n][:, ms], prob[:, n, ms], ident[:, :])
                last.then_inc(pt_done, 1)

            def attend_ctx(b, first):
                pe.wait_ge(pt_ready, TN * (b + 1))
                pe.wait_ge(ctx_ready, KM * (b + 1))
                for e in range(KE):
                    es = slice(e * P, (e + 1) * P)
                    for m in range(KM):
                        last = product(ct_bank[e][:, :], ctx_hi[:, m, es], ctx_lo[:, m, es],
                                       pt_hi[:, m, :], pt_lo[:, m, :], m == 0, m == KM - 1)
                    last.then_inc(ct_done, 1)

            def gate_weights():
                for e in range(KE):
                    es = slice(e * P, (e + 1) * P)
                    for k in range(KD):
                        if e == 0:
                            pe.wait_ge(wg2_ready, k + 1)
                        last = product(wgm_bank[e][:, :], wm_hi[:, k, es], wm_lo[:, k, es],
                                       wg2_hi[:, k, :], wg2_lo[:, k, :], k == 0, k == KD - 1)
                    last.then_inc(wgm_done, 1)

            def gate_c(b, n, e, first):
                ns = slice(n * P, (n + 1) * P)
                if n == 0:
                    pe.wait_ge(ct_ready, KE * b + e + 1)
                    if first:
                        pe.wait_ge(wgm_ready, e + 1)
                last = product(gate[n][:, :], ct_hi[:, e, ns], ct_lo[:, e, ns],
                               wgm_hi[:, e, :], wgm_lo[:, e, :], False, e == KE - 1)
                if e == KE - 1:
                    last.then_inc(gate_done, 1)

            def context(b, i, e, first):
                n, cols = pieces(b)[i]
                ns = slice(n * P, (n + 1) * P)
                if first and i == 0:
                    pe.wait_ge(wmt_ready, e + 1)
                if first and i == 1 and e == 0:
                    pe.wait_ge(wgm_ready, KE)
                if i == TN and e == 0:
                    pe.wait_ge(v_done, TN * b + 2)
                last = product(context_bank[i][:, cols], ct_hi[:, e, ns], ct_lo[:, e, ns],
                               wmt_hi[:, e, cols], wmt_lo[:, e, cols], e == 0, e == KE - 1)
                if e == KE - 1:
                    last.then_inc(context_done, 1)

            def batch(b, first):
                gate_x(b, 0, first)
                if first:
                    gate_x(b, 1, first)
                for n in range(TN):
                    scores(b, n, first)
                if not first:
                    gate_x(b, 1, first)
                    transposes(b, 0)
                    transposes(b, 1)
                    gate_x(b, 2, first)
                else:
                    gate_x(b, 2, first)
                    pe.wait_ge(ident_done, 1)
                    transposes(b, 0)
                    transposes(b, 1)
                transposes(b, 2)
                transposes(b, 3)
                gate_x(b, 3, first)
                attend_ctx(b, first)
                if first:
                    gate_weights()
                gate_c(b, 0, 0, first)
                context(b, 0, 0, first)
                gate_c(b, 1, 0, first)
                gate_c(b, 0, 1, first)
                context(b, 0, 1, first)
                gate_c(b, 1, 1, first)
                context(b, 1, 0, first)
                context(b, 1, 1, first)
                for n in range(2, TN):
                    for e in range(KE):
                        gate_c(b, n, e, first)
                    for i, (tile, _) in enumerate(pieces(b)):
                        if tile == n:
                            for e in range(KE):
                                context(b, i, e, first)

            pe.wait_ge(warm_done, 1)
            for _ in range(WARM_UP):
                nc.tensor.matmul(gate[TN - 1][:, :], warm[:, 0:P], warm[:, :], start=True, stop=True)
            first_xw()
            batch(0, True)
            with pe.Fori(1, B - 1) as b:
                xw(b)
                batch(b, False)
            xw(B - 1)
            batch(B - 1, False)

        @block.vector
        def _(dve):
            def remainder(lo, whole, hi, done):
                nc.vector.tensor_tensor(lo, whole, hi.bitcast(F32), ALU.subtract).then_inc(done, 1)

            nc.vector.memset(warm[:, :], 0.0).then_inc(warm_done, 1)
            for k in range(KD):
                dve.wait_ge(xt_hi_done, k + 1)
                remainder(xt_lo[:, k, :], xt_raw[:, k, :], xt_hi[:, k, :], xt_ready)
                dve.wait_ge(wm_hi_done, k + 1)
                remainder(wm_lo[:, k, :], wm_raw[:, k, :], wm_hi[:, k, :], wm_ready)
            for k in range(KD):
                dve.wait_ge(wg1_hi_done, k + 1)
                remainder(wg1_lo[:, k, :], wgt_raw[:, k, :], wg1_hi[:, k, :], wg1_ready)

            def row_max(b, n):
                dve.wait_ge(scores_done, TN * b + n + 1)
                nc.vector.tensor_reduce(neg_max[:, n:n + 1], tile_bank[n][:, :], AX.X, ALU.max, negate=True)\
                    .then_inc(max_done, 1)

            def normalise(b, n):
                dve.wait_ge(exp_done, TN * b + n + 1)
                nc.vector.reciprocal(inv_sum[:, n:n + 1], row_sum[:, n:n + 1]).then_inc(inv_done, 1)
                dve.wait_ge(inv_done, TN * b + n + 1)
                nc.vector.tensor_scalar(prob[:, n, :], prob[:, n, :], inv_sum[:, n:n + 1], None, ALU.mult)\
                    .then_inc(prob_ready, 1)

            def gate_sum(b, n):
                dve.wait_ge(gate_done, TN * b + n + 1)
                nc.vector.tensor_tensor(z[:, n % 2, :], gate[n][:, :], bias[:, :], ALU.add).then_inc(z_done, 1)

            def gated_context(b, i):
                n, cols = pieces(b)[i]
                dve.wait_ge(tanh_done, TN * b + n + 1)
                dve.wait_ge(context_done, TN * b + i + 1)
                nc.vector.scalar_tensor_tensor(out=v[:, n % 2, cols], in0=z[:, n % 2, cols], scalar=1.0,
                                               in1=context_bank[i][:, cols], op0=ALU.add, op1=ALU.mult)\
                    .then_inc(v_done, 1)

            def fuse(b, i):
                n, cols = pieces(b)[i]
                if i == POOL_FUSED:
                    dve.wait_ge(x_loaded, 16 * (b + 1))
                dve.wait_ge(v_done, TN * b + i + 1)
                nc.vector.tensor_tensor(rows[:, n, cols], v[:, n % 2, cols], rows[:, n, cols], ALU.add)\
                    .then_inc(fused_done, 1)

            def scaled_rows(b, i):
                n, cols = pieces(b)[i]
                dve.wait_ge(rstd_done, TN * b + n + 1)
                nc.vector.scalar_tensor_tensor(out=rows[:, n, cols], in0=rows[:, n, cols],
                                               scalar=rstd[:, n:n + 1], in1=normw[:, cols],
                                               op0=ALU.mult, op1=ALU.mult).then_inc(rows_done, 1)

            def attend(b, first):
                for e in range(KE):
                    dve.wait_ge(xw_hi_done, KE * b + e + 1)
                    nc.vector.scalar_tensor_tensor(out=xw_lo[:, e, :], in0=xw_bank[e][:, :], scalar=SCALE,
                                                   in1=xw_hi[:, e, :].bitcast(F32), op0=ALU.mult,
                                                   op1=ALU.subtract).then_inc(xw_ready, 1)
                row_max(b, 0)
                for n in range(1, TN):
                    row_max(b, n)
                    normalise(b, n - 1)
                normalise(b, TN - 1)
                for n in range(TN):
                    dve.wait_ge(pt_hi_done, TN * b + n + 1)
                    ns = slice(n * P, (n + 1) * P)
                    remainder(pt_lo[:, :, ns], tile_bank[n][:, :].rearrange("p (m j) -> p m j", j=P),
                              pt_hi[:, :, ns], pt_ready)
                if first:
                    for e in range(KE):
                        dve.wait_ge(wmt_hi_done, e + 1)
                        nc.vector.scalar_tensor_tensor(out=wmt_lo[:, e, :], in0=wmt_raw[:, e, :], scalar=0.5,
                                                       in1=wmt_hi[:, e, :].bitcast(F32), op0=ALU.mult,
                                                       op1=ALU.subtract).then_inc(wmt_ready, 1)
                for e in range(KE):
                    dve.wait_ge(ct_hi_done, KE * b + e + 1)
                    remainder(ct_lo[:, e, :], ct_bank[e][:, :], ct_hi[:, e, :], ct_ready)
                if first:
                    for e in range(KE):
                        dve.wait_ge(wgm_done, e + 1)
                        nc.vector.tensor_copy(wgm_hi[:, e, :], wgm_bank[e][:, :]).then_inc(wgm_hi_done, 1)
                        dve.wait_ge(wgm_hi_done, e + 1)
                        remainder(wgm_lo[:, e, :], wgm_bank[e][:, :], wgm_hi[:, e, :], wgm_ready)
                    dve.wait_ge(bias_loaded, 16)
                    dve.wait_ge(normw_loaded, 16)
                gate_sum(b, 0)
                gated_context(b, 0)
                gate_sum(b, 1)
                gated_context(b, 1)
                gate_sum(b, 2)
                gated_context(b, 2)
                gate_sum(b, 3)
                scaled_rows(b, 0)
                for i in range(3, len(pieces(b))):
                    gated_context(b, i)
                for i in range(3, len(pieces(b))):
                    fuse(b, i)
                for i in range(1, len(pieces(b))):
                    scaled_rows(b, i)

            attend(0, True)
            with dve.Fori(1, B - 1) as b:
                attend(b, False)
            attend(B - 1, False)


def kernel(x, ctx_1024, L0_xattn_W_mem, L0_xattn_W_gate, L0_xattn_b_gate, L0_xattn_norm_w):
    import numpy as _np
    import concourse.bacc as _bacc
    from concourse import mybir as _mybir
    from concourse.bass_utils import run_bass_kernel_spmd as _run

    x, ctx, w_mem, w_gate = (_np.asarray(a) for a in (x, ctx_1024, L0_xattn_W_mem, L0_xattn_W_gate))

    def over_partitions(a):
        return _np.ascontiguousarray(a.reshape(*a.shape[:-2], -1, 128, a.shape[-1]).swapaxes(-3, -2))

    arrays = {
        "x_dram": _np.ascontiguousarray(x),
        "x_t_dram": over_partitions(x.swapaxes(1, 2)),
        "ctx_dram": over_partitions(ctx),
        "ctx_t_dram": over_partitions(ctx.swapaxes(1, 2)),
        "w_mem_dram": over_partitions(w_mem),
        "w_mem_t_dram": over_partitions(w_mem.T),
        "w_gate_t_dram": over_partitions(w_gate.T),
        "b_gate_dram": _np.ascontiguousarray(L0_xattn_b_gate),
        "norm_w_dram": _np.ascontiguousarray(L0_xattn_norm_w),
    }
    nc = _bacc.Bacc("TRN2", target_bir_lowering=False, num_devices=1)
    args = [nc.dram_tensor(n, a.shape, _mybir.dt.from_np(a.dtype), kind="ExternalInput").ap()
            for n, a in arrays.items()]
    args.append(nc.dram_tensor("out_dram", x.shape, _mybir.dt.float32, kind="ExternalOutput").ap())
    bass_gated_cross_attention(nc, *args)
    r = _run(nc, [arrays], core_ids=[0])
    return r.results[0]["out_dram"]
```
